# Optimizing a Trainium2 kernel written in Bass

```python
import numpy as np
import jax
import jax.numpy as jnp

def _softmax(x, axis=-1):
    return jax.nn.softmax(x, axis=axis)
def _gelu(x):
    return jax.nn.gelu(x, approximate=True)
def _silu(x):
    return jax.nn.silu(x)
def _sigmoid(x):
    return jax.nn.sigmoid(x)
def _layernorm(x, axis=-1, eps=1e-5):
    m = jnp.mean(x, axis=axis, keepdims=True)
    v = jnp.var(x, axis=axis, keepdims=True)
    return (x - m) / jnp.sqrt(v + eps)
def _scatter_add(tgt, idx, src, axis=0):
    return tgt.at[idx].add(src)
def _segment_sum(src, seg, n):
    return jax.ops.segment_sum(src, seg, n)

kernel_name = 'mk_conv_preact_d1_conv_nhwc64_936563'

def setup_inputs(seed: int = 0):
    np.random.seed(seed)
    _w = jnp.asarray
    def _rec_inputs():
        import jax
        import jax.numpy as jnp
        _gk = jax.random.key(seed)
        x = -1.504e-05 + 0.9999 * jax.random.normal(jax.random.fold_in(_gk, 1), (1024, 64, 14, 64), jnp.float32)
        return x
    x = _rec_inputs()
    def _L0_conv_setup():
        import jax, jax.numpy as jnp
        import numpy as np
        EMB = 64
        SEQ = 14
        C = 64
        B = 1024
        LN_EPS = 1e-05
        key = jax.random.key(seed)
        ks = jax.random.split(key, 8)
        s = 1.0 / np.sqrt(EMB)
        return {'x': jax.random.normal(ks[0], (B, C, SEQ, EMB), dtype=jnp.float32), 'w_c': jax.random.normal(ks[1], (SEQ, SEQ), dtype=jnp.float32) * (1.0 / np.sqrt(SEQ)), 'Wq': jax.random.normal(ks[2], (EMB, EMB), dtype=jnp.float32) * s, 'bq': jax.random.normal(ks[3], (EMB,), dtype=jnp.float32) * 0.01, 'Wk': jax.random.normal(ks[4], (EMB, EMB), dtype=jnp.float32) * s, 'bk': jax.random.normal(ks[5], (EMB,), dtype=jnp.float32) * 0.01, 'Wv': jax.random.normal(ks[6], (EMB, EMB), dtype=jnp.float32) * s, 'bv': jax.random.normal(ks[7], (EMB,), dtype=jnp.float32) * 0.01, 'ln_g': jnp.ones((SEQ,), dtype=jnp.float32), 'ln_b': jnp.zeros((SEQ,), dtype=jnp.float32)}
    _L0_conv_all = _L0_conv_setup()
    _L0_conv_in = {k: v for k, v in _L0_conv_all.items() if k in ('w_c', 'Wq', 'bq', 'Wk', 'bk', 'Wv', 'bv', 'ln_g', 'ln_b', )}
    del _L0_conv_all

    return {
        "x": x,
        "L0_conv_w_c": _L0_conv_in["w_c"],
        "L0_conv_Wq": _L0_conv_in["Wq"],
        "L0_conv_bq": _L0_conv_in["bq"],
        "L0_conv_Wk": _L0_conv_in["Wk"],
        "L0_conv_bk": _L0_conv_in["bk"],
        "L0_conv_Wv": _L0_conv_in["Wv"],
        "L0_conv_bv": _L0_conv_in["bv"],
        "L0_conv_ln_g": _L0_conv_in["ln_g"],
        "L0_conv_ln_b": _L0_conv_in["ln_b"],
    }

def reference(x, L0_conv_w_c, L0_conv_Wq, L0_conv_bq, L0_conv_Wk, L0_conv_bk, L0_conv_Wv, L0_conv_bv, L0_conv_ln_g, L0_conv_ln_b):
    import jax
    import jax.numpy as jnp
    def _L0_conv_ref(x, w_c, Wq, bq, Wk, bk, Wv, bv, ln_g, ln_b):
        import jax, jax.numpy as jnp
        import numpy as np
        EMB = 64
        SEQ = 14
        C = 64
        B = 1024
        LN_EPS = 1e-05
        q = jnp.einsum('bcqd,ed->bcqe', x, Wq) + bq
        k = jnp.einsum('bcqd,ed->bcqe', x, Wk) + bk
        v = jnp.einsum('bcqd,ed->bcqe', x, Wv) + bv
        energy = jnp.einsum('bcqd,bckd->bcqk', q, k)
        energy1 = jnp.einsum('al,bclv->bcav', w_c, energy)
        mu = jnp.mean(energy1, axis=-1, keepdims=True)
        var = jnp.mean(jnp.square(energy1 - mu), axis=-1, keepdims=True)
        energy1 = (energy1 - mu) * jax.lax.rsqrt(var + LN_EPS) * ln_g + ln_b
        scaling = EMB ** 0.5
        att = jax.nn.softmax(energy1 / scaling, axis=-1)
        out = jnp.einsum('bcal,bclv->bcav', att, v)
        return out

    def _gn(v, G=32, eps=1e-5):
        B_, H_, W_, C_ = v.shape
        g = v.reshape(B_, H_, W_, G, C_ // G)
        m = jnp.mean(g, axis=(1, 2, 4), keepdims=True)
        s = jnp.var(g, axis=(1, 2, 4), keepdims=True)
        return ((g - m) / jnp.sqrt(s + eps)).reshape(v.shape)

    def _ln_c(v, eps=1e-6):
        m = jnp.mean(v, axis=-1, keepdims=True)
        s = jnp.var(v, axis=-1, keepdims=True)
        return (v - m) / jnp.sqrt(s + eps)

    def _ln_t(v, eps=1e-5):
        m = jnp.mean(v, axis=-1, keepdims=True)
        s = jnp.var(v, axis=-1, keepdims=True)
        return (v - m) / jnp.sqrt(s + eps)

    def _to_tokens(v):
        B_, H_, W_, C_ = v.shape
        return v.reshape(B_, H_ * W_, C_)
    def _from_tokens(t, like):
        return t.reshape(like.shape)

    x = x + _L0_conv_ref(_gn(x), L0_conv_w_c, L0_conv_Wq, L0_conv_bq, L0_conv_Wk, L0_conv_bk, L0_conv_Wv, L0_conv_bv, L0_conv_ln_g, L0_conv_ln_b)
    return x


_drawn_inputs = setup_inputs


def setup_inputs(seed=0):
    import zlib

    import numpy as np

    out = dict(_drawn_inputs(seed))
    spreads = {'L0_conv_ln_g': (1.0, 0.6), 'L0_conv_ln_b': (0.0, 2.0)}
    factors = {'L0_conv_bq': 57.636, 'L0_conv_bk': 64.0, 'L0_conv_bv': 5.651}
    for name, (base, spread) in spreads.items():
        noise = np.random.default_rng([zlib.crc32(name.encode()), seed]).standard_normal(out[name].shape)
        drawn = base * np.exp(spread * noise) if base else spread * noise
        out[name] = jnp.asarray(drawn.astype(out[name].dtype))
    for name, factor in factors.items():
        out[name] = (out[name] * factor).astype(out[name].dtype)
    return out
```

```python
from contextlib import ExitStack

import concourse.bass as bass
from concourse import mybir

F32 = mybir.dt.float32
ALU = mybir.AluOpType
ACT = mybir.ActivationFunctionType
AX_X = mybir.AxisListType.X

P = 128
QUAD = 32
QUADS = P // QUAD
PAIR = 2
SETS = 2
SLOTS = 4
GN_EPS = 1e-5
LN_EPS = 1e-5


def conv_preact_kernel(nc, x, w_c, Wq, bq, Wk, bk, Wv, bv, ln_g, ln_b, ident_c, group_c, half_c, out):
    B, C, SEQ, EMB = x.shape
    ROWS = PAIR * SEQ
    G = C // (QUADS * PAIR)
    G2 = G // 2
    TCOLS = G2 * QUADS * ROWS
    GC = QUADS * ROWS
    NP = B // SETS
    BG = SETS * G
    SCALE = float(EMB) ** -0.5
    assert 2 * EMB == P and ROWS <= QUAD and NP % SLOTS == 0

    x_dram = x.rearrange("b (g r s) q d -> r (s q) b g d", g=G, r=QUADS)
    out_dram = out.rearrange("b (g r s) q d -> r (s q) b g d", g=G, r=QUADS)

    with ExitStack() as ctx:
        def sb(name, shape):
            return ctx.enter_context(nc.sbuf_tensor(name, shape, F32))

        def psum(name, shape):
            return ctx.enter_context(nc.psum_tensor(name, shape, F32))

        def sem(name):
            return ctx.enter_context(nc.semaphore(name))

        ident = sb("ident", [P, P])
        group_mean = sb("group_mean", [P, P])
        half = sb("half", [P, PAIR])
        half_all = sb("half_all", [P, BG, PAIR])
        wq_sb = sb("wq_sb", [EMB, EMB])
        wk_sb = sb("wk_sb", [EMB, EMB])
        wv_sb = sb("wv_sb", [EMB, EMB])
        bq_sb = sb("bq_sb", [EMB, 1])
        a_bd = sb("a_bd", [P, P])
        wv_bd = sb("wv_bd", [P, P])
        w_col = sb("w_col", [P, 1])
        mix = sb("mix", [P, PAIR, P])
        g_row = sb("g_row", [P, SEQ])
        b_row = sb("b_row", [P, SEQ])
        bv_row = sb("bv_row", [P, EMB])
        g_all = sb("g_all", [P, BG, SEQ])
        b_all = sb("b_all", [P, BG, SEQ])
        bv_all = sb("bv_all", [P, BG, EMB])
        minus_half = sb("minus_half", [P, BG])

        xs = sb("xs", [P, SLOTS, SETS, G, EMB])
        res = sb("res", [P, SLOTS, SETS, G, EMB])
        xnt = sb("xnt", [P, SETS, TCOLS])
        ht = sb("ht", [P, SETS, TCOLS + QUAD - ROWS])
        bns = sb("bns", [P, SETS, 6])
        st = sb("st", [P, SETS, 2])
        st_sq = sb("st_sq", [P, SETS])
        gm = sb("gm", [P, SETS, 2])
        gm_sq = sb("gm_sq", [P, SETS])
        gvar = sb("gvar", [P, SETS])
        gve = sb("gve", [P, SETS])
        gneg = sb("gneg", [P, SETS])
        gscale = sb("gscale", [P, SLOTS, SETS])
        gshift = sb("gshift", [P, SLOTS, SETS])
        en = sb("en", [P, SETS, G2, 2, ROWS])
        esum = sb("esum", [P, BG])
        cent = sb("cent", [P, BG, SEQ])
        cg = sb("cg", [P, BG, SEQ])
        sq = sb("sq", [P, BG, SEQ])
        ssum = sb("ssum", [P, BG])
        lve = sb("lve", [P, BG])
        lrs = sb("lrs", [P, BG])
        t1 = sb("t1", [P, BG, SEQ])
        t2 = sb("t2", [P, BG, SEQ])
        tmax = sb("tmax", [P, BG])
        t3 = sb("t3", [P, BG, SEQ])
        ex = sb("ex", [P, BG, SEQ])
        den = sb("den", [P, BG])
        rden = sb("rden", [P, BG])
        rden_s = sb("rden_s", [P, BG, PAIR])
        att = sb("att", [P, BG, QUAD])
        att_bd = sb("att_bd", [P, BG, QUADS, QUAD])
        znt = sb("znt", [P, SETS, G2, QUADS * QUAD])

        ps_x = [psum(f"ps_x{b}", [P, G2, QUADS, QUAD]) for b in range(SETS)]
        ps_h = psum("ps_h", [P, 512])
        ps_e = [psum(f"ps_e{h}", [P, SETS * G2, ROWS]) for h in range(2)]
        ps_m = psum("ps_m", [P, BG, SEQ])
        ps_z = psum("ps_z", [P, G2, QUADS * QUAD])
        ps_o = psum("ps_o", [P, 512])

        const_loaded = sem("const_loaded")
        cleared = sem("cleared")
        expanded = sem("expanded")
        weights_mm = sem("weights_mm")
        weights_done = sem("weights_done")
        x_loaded = [sem(f"x_loaded{k}") for k in range(SLOTS)]
        stored = [sem(f"stored{k}") for k in range(SLOTS)]
        xt_ready = sem("xt_ready")
        bn_ready = sem("bn_ready")
        agg_ready = sem("agg_ready")
        stsq_ready = sem("stsq_ready")
        st_ready = sem("st_ready")
        gm_mm = sem("gm_mm")
        gm_ready = sem("gm_ready")
        gmsq_ready = sem("gmsq_ready")
        gvar_ready = sem("gvar_ready")
        gve_ready = sem("gve_ready")
        gneg_ready = sem("gneg_ready")
        gscale_ready = sem("gscale_ready")
        gshift_ready = sem("gshift_ready")
        xn_ready = sem("xn_ready")
        h_mm = sem("h_mm")
        ht_ready = sem("ht_ready")
        e_mm = sem("e_mm")
        en_ready = sem("en_ready")
        mix_mm = sem("mix_mm")
        esum_ready = sem("esum_ready")
        cent_ready = sem("cent_ready")
        cg_ready = sem("cg_ready")
        sq_ready = sem("sq_ready")
        ssum_ready = sem("ssum_ready")
        lve_ready = sem("lve_ready")
        lrs_ready = sem("lrs_ready")
        t1_ready = sem("t1_ready")
        t2_ready = sem("t2_ready")
        tmax_ready = sem("tmax_ready")
        t3_ready = sem("t3_ready")
        ex_ready = sem("ex_ready")
        den_ready = sem("den_ready")
        rden_ready = sem("rden_ready")
        rdens_ready = sem("rdens_ready")
        att_ready = sem("att_ready")
        bd_ready = sem("bd_ready")
        z_mm = sem("z_mm")
        zn_ready = sem("zn_ready")
        o_mm = sem("o_mm")
        xb_ready = sem("xb_ready")
        res_ready = sem("res_ready")

        CONSTS = 10 + QUADS * PAIR
        LOAD = 16 * QUADS

        block = ctx.enter_context(nc.Block())

        def after(eng, semaphore, value):
            if isinstance(value, int) and value <= 0:
                return
            eng.wait_ge(semaphore, value)

        def steps(eng, first, step):
            for p in range(first, SLOTS):
                step(p, p % SLOTS)
            with eng.Fori(SLOTS, NP - 2 * SLOTS + 1, SLOTS) as base:
                for k in range(SLOTS):
                    step(base + k, k)
            for p in range(NP - SLOTS, NP + 1):
                step(p, p % SLOTS)

        def has(p):
            return not isinstance(p, int) or 0 <= p < NP

        def fills(p, k):
            if isinstance(p, int):
                return (p // SLOTS + 1) * LOAD
            return (p - k) * (LOAD // SLOTS) + LOAD

        @block.sync
        def _(sp):
            for dst, src in ((ident[:], ident_c), (group_mean[:], group_c), (half[:], half_c),
                             (wq_sb[:], Wq), (wk_sb[:], Wk), (wv_sb[:], Wv),
                             (bq_sb[:], bq.rearrange("(e a) -> e a", a=1)),
                             (g_row[:], ln_g.partition_broadcast(P)),
                             (b_row[:], ln_b.partition_broadcast(P)),
                             (bv_row[:], bv.partition_broadcast(P))):
                sp.dma_start(dst, src).then_inc(const_loaded, 16)
            sp.wait_ge(cleared, 6)
            for r in range(QUADS):
                for s in range(PAIR):
                    lo = QUAD * r + SEQ * s
                    sp.dma_start(mix[lo:lo + SEQ, s, lo:lo + SEQ],
                                 w_c.rearrange("a l -> l a"),
                                 allow_slow_non_contiguous=True).then_inc(const_loaded, 16)

            def load(p, k):
                for r in range(QUADS):
                    sp.dma_start(xs[QUAD * r:QUAD * r + ROWS, k],
                                 x_dram[r, :, bass.ds(p * SETS, SETS)]).then_inc(x_loaded[k], 16)

            for p in range(SLOTS - 1):
                load(p, p)

            def step(p, k):
                nk = (k + SLOTS - 1) % SLOTS
                after(sp, z_mm, SETS * p)
                after(sp, xb_ready, p)
                if has(p + SLOTS - 1):
                    load(p + SLOTS - 1, nk)
                if has(p - 1):
                    sp.wait_ge(res_ready, SETS * p)
                    for r in range(QUADS):
                        sp.dma_start(out_dram[r, :, bass.ds((p - 1) * SETS, SETS)],
                                     res[QUAD * r:QUAD * r + ROWS, nk]).then_inc(stored[nk], 16)

            steps(sp, 0, step)
            for k in range(SLOTS):
                sp.wait_ge(stored[k], NP // SLOTS * LOAD)

        @block.gpsimd
        def _(pool):
            nc.gpsimd.memset(xs[:], 0.0).then_inc(cleared, 1)
            nc.gpsimd.memset(mix[:], 0.0).then_inc(cleared, 1)
            nc.gpsimd.memset(att_bd[:], 0.0).then_inc(cleared, 1)
            nc.gpsimd.memset(att[:], 0.0).then_inc(cleared, 1)
            nc.gpsimd.memset(ht[:], 0.0).then_inc(cleared, 1)
            nc.gpsimd.memset(minus_half[:], -0.5).then_inc(cleared, 1)
            pool.wait_ge(const_loaded, 16 * CONSTS)
            for n in range(BG):
                nc.gpsimd.tensor_scalar(g_all[:, n], g_row[:], SCALE, None, ALU.mult).then_inc(expanded, 1)
                nc.gpsimd.tensor_scalar(b_all[:, n], b_row[:], SCALE, None, ALU.mult).then_inc(expanded, 1)
                nc.gpsimd.tensor_copy(bv_all[:, n], bv_row[:]).then_inc(expanded, 1)
                nc.gpsimd.tensor_copy(half_all[:, n], half[:]).then_inc(expanded, 1)
            pool.wait_ge(expanded, 4 * BG)

            def over_keys(a):
                return a.unsqueeze(2).to_broadcast([P, BG, SEQ])

            def step(p, k):
                if has(p + 1):
                    n = (k + 1) % SLOTS
                if has(p):
                    pool.wait_ge(x_loaded[k], fills(p, k))
                    after(pool, stored[k], fills(p - SLOTS, k))
                    nc.gpsimd.tensor_tensor(res[:, k].rearrange("p b g d -> p (b g) d"),
                                            xs[:, k].rearrange("p b g d -> p (b g) d"),
                                            bv_all[:], ALU.add).then_inc(xb_ready, 1)
                    pool.wait_ge(cent_ready, p + 1)
                    after(pool, ssum_ready, p)
                    nc.gpsimd.tensor_tensor(sq[:], cent[:], cent[:], ALU.mult).then_inc(sq_ready, 1)
                    after(pool, t1_ready, p)
                    nc.gpsimd.tensor_tensor(cg[:], cent[:], g_all[:], ALU.mult).then_inc(cg_ready, 1)
                if has(p + 1):
                    pool.wait_ge(gve_ready, p + 2)
                    after(pool, zn_ready, SETS * (p + 2 - SLOTS))
                    nc.gpsimd.tensor_tensor(gscale[:, n], gve[:], minus_half[:, 0:SETS],
                                            ALU.pow).then_inc(gscale_ready, 1)
                    pool.wait_ge(gscale_ready, p + 2)
                    pool.wait_ge(gneg_ready, p + 2)
                    nc.gpsimd.tensor_tensor(gshift[:, n], gneg[:], gscale[:, n],
                                            ALU.mult).then_inc(gshift_ready, 1)
                if has(p):
                    pool.wait_ge(lve_ready, p + 1)
                    nc.gpsimd.tensor_tensor(lrs[:], lve[:], minus_half[:], ALU.pow).then_inc(lrs_ready, 1)
                    pool.wait_ge(cg_ready, p + 1)
                    pool.wait_ge(lrs_ready, p + 1)
                    nc.gpsimd.tensor_tensor(t1[:], cg[:], over_keys(lrs[:]), ALU.mult).then_inc(t1_ready, 1)
                    pool.wait_ge(t1_ready, p + 1)
                    nc.gpsimd.tensor_tensor(t2[:], t1[:], b_all[:], ALU.add).then_inc(t2_ready, 1)
                    pool.wait_ge(t2_ready, p + 1)
                    pool.wait_ge(tmax_ready, p + 1)
                    after(pool, ex_ready, p)
                    nc.gpsimd.tensor_tensor(t3[:], t2[:], over_keys(tmax[:]), ALU.subtract).then_inc(t3_ready, 1)
                    pool.wait_ge(rden_ready, p + 1)
                    nc.gpsimd.tensor_tensor(rden_s[:], rden[:].unsqueeze(2).to_broadcast([P, BG, PAIR]),
                                            half_all[:], ALU.mult).then_inc(rdens_ready, 1)
                    pool.wait_ge(rdens_ready, p + 1)
                    after(pool, bd_ready, p)
                    nc.gpsimd.tensor_tensor(
                        att[:, :, 0:ROWS].rearrange("p n (s k) -> p n s k", s=PAIR),
                        ex[:].unsqueeze(2).to_broadcast([P, BG, PAIR, SEQ]),
                        rden_s[:].unsqueeze(3).to_broadcast([P, BG, PAIR, SEQ]),
                        ALU.mult).then_inc(att_ready, 1)

            steps(pool, -1, step)

        @block.scalar
        def _(act):
            def normalised(dst, src, k, b):
                return nc.scalar.activation(dst, src, ACT.Identity, bias=gshift[:, k, b:b + 1],
                                            scale=gscale[:, k, b:b + 1])

            def h_out(p, b):
                act.wait_ge(h_mm, SETS * p + b + 1)
                nc.scalar.activation(ht[:, b, 0:TCOLS], ps_h[:, 0:TCOLS], ACT.Identity,
                                     bias=w_col[:, 0:1]).then_inc(ht_ready, 1)

            act.wait_ge(cleared, 6)
            act.wait_ge(weights_done, 5)

            def step(p, k):
                n, last = (k + 1) % SLOTS, (k + SLOTS - 1) % SLOTS
                if has(p):
                    act.wait_ge(e_mm, p + 1)
                    after(act, mix_mm, p)
                    for h in range(2):
                        nc.scalar.activation(en[:, :, :, h].rearrange("p b g k -> p (b g) k"), ps_e[h][:],
                                             ACT.Copy).then_inc(en_ready, 1)
                if has(p - 1):
                    for b in range(SETS):
                        act.wait_ge(z_mm, SETS * (p - 1) + b + 1)
                        after(act, o_mm, SETS * (p - 2) + b + 1)
                        normalised(znt[:, b, :, :], ps_z[:], last, b).then_inc(zn_ready, 1)
                if has(p + 1):
                    act.wait_ge(gshift_ready, p + 2)
                    for b in range(SETS):
                        normalised(xnt[:, b].rearrange("p (g r c) -> p g r c", g=G2, r=QUADS),
                                   ps_x[b][:, :, :, 0:ROWS], n, b).then_inc(xn_ready, 1)
                    h_out(p + 1, 0)
                if has(p):
                    act.wait_ge(t3_ready, p + 1)
                    after(act, att_ready, p)
                    nc.scalar.activation(ex[:], t3[:], ACT.Exp).then_inc(ex_ready, 1)
                if has(p + 1):
                    h_out(p + 1, 1)

            steps(act, -1, step)

        @block.vector
        def _(dve):
            nc.vector.memset(a_bd[:], 0.0).then_inc(weights_done, 1)
            nc.vector.memset(wv_bd[:], 0.0).then_inc(weights_done, 1)
            dve.wait_ge(weights_done, 2)
            dve.wait_ge(weights_mm, 6)
            nc.vector.tensor_copy(w_col[:], ps_h[:, P:P + 1]).then_inc(weights_done, 1)
            for h in range(2):
                r = slice(EMB * h, EMB * h + EMB)
                a = nc.vector.tensor_copy(a_bd[r, r], ps_h[r, 0:EMB])
                v = nc.vector.tensor_copy(wv_bd[r, r], ps_h[r, EMB:2 * EMB])
                v.then_inc(weights_done, 1)

            def result(p, k, b):
                dve.wait_ge(o_mm, SETS * p + b + 1)
                dve.wait_ge(xb_ready, p + 1)
                r = res[:, k, b].rearrange("p g d -> p (g d)")
                nc.vector.tensor_tensor(r, ps_o[:], r, ALU.add).then_inc(res_ready, 1)

            def step(p, k):
                last = (k + SLOTS - 1) % SLOTS
                if has(p + 1):
                    for b in range(SETS):
                        dve.wait_ge(xt_ready, SETS * (p + 1) + b + 1)
                        nc.vector.bn_stats(bns[:, b], ps_x[b][:, :, :, 0:ROWS]).then_inc(bn_ready, 1)
                if has(p):
                    dve.wait_ge(mix_mm, p + 1)
                    if has(p + 1):
                        dve.wait_ge(bn_ready, SETS * (p + 2))
                    nc.vector.reduce_sum(esum[:], ps_m[:], AX_X).then_inc(esum_ready, 1)
                elif has(p + 1):
                    dve.wait_ge(bn_ready, SETS * (p + 2))
                if has(p + 1):
                    for b in range(SETS):
                        nc.vector.bn_aggr(st[:, b], bns[:, b]).then_inc(agg_ready, 1)
                    dve.wait_ge(agg_ready, SETS * (p + 2))
                    nc.vector.tensor_tensor(st_sq[:], st[:, :, 0], st[:, :, 0], ALU.mult).then_inc(stsq_ready, 1)
                    dve.wait_ge(stsq_ready, p + 2)
                    nc.vector.tensor_tensor(st[:, :, 1], st[:, :, 1], st_sq[:], ALU.add).then_inc(st_ready, 1)
                if has(p):
                    dve.wait_ge(esum_ready, p + 1)
                    after(dve, cg_ready, p)
                    nc.vector.scalar_tensor_tensor(
                        out=cent[:], in0=esum[:].unsqueeze(2).to_broadcast([P, BG, SEQ]), scalar=-1.0 / SEQ,
                        in1=ps_m[:], op0=ALU.mult, op1=ALU.add).then_inc(cent_ready, 1)
                if has(p + 1):
                    dve.wait_ge(gm_mm, p + 2)
                    nc.vector.tensor_copy(gm[:].rearrange("p b t -> p (b t)"),
                                          ps_h[:, 0:2 * SETS]).then_inc(gm_ready, 1)
                    dve.wait_ge(gm_ready, p + 2)
                    nc.vector.tensor_tensor(gm_sq[:], gm[:, :, 0], gm[:, :, 0], ALU.mult).then_inc(gmsq_ready, 1)
                    dve.wait_ge(gmsq_ready, p + 2)
                    nc.vector.tensor_tensor(gvar[:], gm[:, :, 1], gm_sq[:], ALU.subtract).then_inc(gvar_ready, 1)
                    dve.wait_ge(gvar_ready, p + 2)
                    after(dve, gshift_ready, p + 1)
                    nc.vector.tensor_scalar(gve[:], gvar[:], 0.0, GN_EPS, ALU.max, ALU.add).then_inc(gve_ready, 1)
                    nc.vector.tensor_scalar(gneg[:], gm[:, :, 0], -1.0, None, ALU.mult).then_inc(gneg_ready, 1)
                if has(p):
                    dve.wait_ge(sq_ready, p + 1)
                    nc.vector.reduce_sum(ssum[:], sq[:], AX_X).then_inc(ssum_ready, 1)
                    dve.wait_ge(ssum_ready, p + 1)
                    after(dve, lrs_ready, p)
                    nc.vector.tensor_scalar(lve[:], ssum[:], 1.0 / SEQ, LN_EPS, ALU.mult,
                                            ALU.add).then_inc(lve_ready, 1)
                if has(p - 1):
                    result(p - 1, last, 0)
                if has(p):
                    dve.wait_ge(t2_ready, p + 1)
                    after(dve, t3_ready, p)
                    nc.vector.reduce_max(tmax[:], t2[:], AX_X).then_inc(tmax_ready, 1)
                if has(p - 1):
                    result(p - 1, last, 1)
                if has(p):
                    dve.wait_ge(ex_ready, p + 1)
                    nc.vector.reduce_sum(den[:], ex[:], AX_X).then_inc(den_ready, 1)
                    dve.wait_ge(den_ready, p + 1)
                    after(dve, rdens_ready, p)
                    nc.vector.reciprocal(rden[:], den[:]).then_inc(rden_ready, 1)
                    dve.wait_ge(att_ready, p + 1)
                    after(dve, z_mm, SETS * p)
                    for r in range(QUADS):
                        q = slice(QUAD * r, QUAD * r + QUAD)
                        bd = nc.vector.transpose(att_bd[q, :, r, :], att[q, :, :])
                    bd.then_inc(bd_ready, 1)

            steps(dve, -1, step)

        @block.tensor
        def _(pe):
            pe.wait_ge(const_loaded, 16 * CONSTS)
            for h in range(2):
                r = slice(EMB * h, EMB * h + EMB)
                nc.tensor.matmul(ps_h[r, 0:EMB], wq_sb[:], wk_sb[:], start=True, stop=True).then_inc(weights_mm, 1)
                nc.tensor.matmul(ps_h[r, EMB:2 * EMB], wv_sb[:], ident[0:EMB, 0:EMB],
                                 start=True, stop=True).then_inc(weights_mm, 1)
                nc.tensor.matmul(ps_h[r, P:P + 1], wk_sb[:], bq_sb[:], start=True, stop=True).then_inc(weights_mm, 1)
            pe.wait_ge(weights_done, 5)
            pe.wait_ge(cleared, 6)

            def energies(p, b):
                for g in range(G2):
                    for r in range(QUADS):
                        c = g * GC + r * ROWS
                        for h in range(2):
                            d = slice(EMB * h, EMB * h + EMB)
                            e = nc.tensor.matmul(ps_e[h][QUAD * r:QUAD * r + QUAD, b * G2 + g, :],
                                                 ht[d, b, c:c + QUAD], xnt[d, b, c:c + ROWS],
                                                 start=True, stop=True)
                if b == SETS - 1:
                    e.then_inc(e_mm, 1)

            def transposed(p, k, b):
                if b == 0:
                    pe.wait_ge(x_loaded[k], fills(p, k))
                after(pe, ht_ready, SETS * p)
                after(pe, xn_ready, SETS * (p - 1) + b + 1)
                for g in range(G2):
                    t = nc.tensor.transpose(ps_x[b][:, g].rearrange("p r c -> p (r c)"),
                                            xs[:, k, b, 2 * g:2 * g + 2].rearrange("p g d -> p (g d)"),
                                            ident[:])
                t.then_inc(xt_ready, 1)

            def mixing(p):
                pe.wait_ge(en_ready, 2 * (p + 1))
                after(pe, cent_ready, p)
                for s in range(PAIR):
                    m = nc.tensor.matmul(
                        ps_m[:], mix[:, s],
                        en[:].rearrange("p b g h (s k) -> p (b g h) s k", s=PAIR)[:, :, s],
                        start=(s == 0), stop=(s == PAIR - 1))
                m.then_inc(mix_mm, 1)

            def group_means(p):
                pe.wait_ge(st_ready, p + 1)
                after(pe, ht_ready, SETS * p)
                nc.tensor.matmul(ps_h[:, 0:2 * SETS], group_mean[:], st[:].rearrange("p b t -> p (b t)"),
                                 start=True, stop=True).then_inc(gm_mm, 1)

            def hidden(p, b):
                pe.wait_ge(xn_ready, SETS * p + b + 1)
                after(pe, ht_ready, SETS * p + b)
                nc.tensor.matmul(ps_h[:, 0:TCOLS], a_bd[:], xnt[:, b], start=True, stop=True).then_inc(h_mm, 1)

            def attend(p, k, b):
                if b == 0:
                    pe.wait_ge(bd_ready, p + 1)
                after(pe, zn_ready, SETS * p + b)
                for g in range(G2):
                    for h in range(2):
                        z = nc.tensor.matmul(ps_z[EMB * h:EMB * h + EMB, g],
                                             xs[:, k, b, 2 * g + h],
                                             att_bd[:, b * G + 2 * g + h].rearrange("p r c -> p (r c)"),
                                             start=True, stop=True)
                z.then_inc(z_mm, 1)

            def values(p, b):
                pe.wait_ge(zn_ready, SETS * p + b + 1)
                after(pe, res_ready, SETS * p + b)
                for g in range(G2):
                    o = nc.tensor.matmul(ps_o[:, g * P:(g + 1) * P], znt[:, b, g], wv_bd[:], start=True, stop=True)
                o.then_inc(o_mm, 1)

            def step(p, k):
                n, last = (k + 1) % SLOTS, (k + SLOTS - 1) % SLOTS
                if has(p) and not has(p + 1):
                    pe.wait_ge(ht_ready, SETS * (p + 1))
                for b in range(SETS):
                    if has(p):
                        energies(p, b)
                    if has(p + 1):
                        transposed(p + 1, n, b)
                if has(p):
                    mixing(p)
                if has(p - 1):
                    attend(p - 1, last, 0)
                if has(p + 1):
                    group_means(p + 1)
                if has(p - 1):
                    attend(p - 1, last, 1)
                    values(p - 1, 0)
                if has(p + 1):
                    hidden(p + 1, 0)
                if has(p - 1):
                    values(p - 1, 1)
                if has(p + 1):
                    hidden(p + 1, 1)

            steps(pe, -1, step)


_INS = ["x", "L0_conv_w_c", "L0_conv_Wq", "L0_conv_bq", "L0_conv_Wk", "L0_conv_bk", "L0_conv_Wv", "L0_conv_bv",
        "L0_conv_ln_g", "L0_conv_ln_b"]


def kernel(**inputs):
    import numpy as _np
    import concourse.bacc as _bacc
    from concourse import mybir as _mybir
    from concourse.bass_utils import run_bass_kernel_spmd as _run

    nc = _bacc.Bacc("TRN2", target_bir_lowering=False, num_devices=1)
    arrays, args = {}, []

    def add(name, a):
        arrays[name] = a
        args.append(nc.dram_tensor(name, a.shape, _mybir.dt.from_np(a.dtype), kind="ExternalInput").ap())

    for name in _INS:
        add(f"in_{name}_dram", _np.ascontiguousarray(inputs[name]))
    seq, emb = inputs["x"].shape[2:]
    p = _np.arange(P)
    add("ident_dram", _np.eye(P, dtype=_np.float32))
    same = (p[:, None] % emb) // 2 == (p[None, :] % emb) // 2
    add("group_dram", same.astype(_np.float32) / _np.float32(4))
    row = p % QUAD
    add("half_dram", _np.stack([(row // seq == s) for s in range(PAIR)], 1).astype(_np.float32))
    shape = inputs["x"].shape
    args.append(nc.dram_tensor("out_0_dram", shape, F32, kind="ExternalOutput").ap())
    conv_preact_kernel(nc, *args)
    r = _run(nc, [arrays], core_ids=[0])
    return r.results[0]["out_0_dram"]
```

```python
from contextlib import ExitStack

import concourse.bass as bass
from concourse import mybir

F32 = mybir.dt.float32
ALU = mybir.AluOpType
ACT = mybir.ActivationFunctionType
AX_X = mybir.AxisListType.X

P = 128
QUAD = 32
QUADS = P // QUAD
PAIR = 2
SETS = 2
SLOTS = 6
LAG = 2
AHEAD = SLOTS - LAG
GN_EPS = 1e-5
LN_EPS = 1e-5


def conv_preact_kernel(nc, x, w_c, Wq, bq, Wk, bk, Wv, bv, ln_g, ln_b, ident_c, group_c, half_c, out):
    B, C, SEQ, EMB = x.shape
    ROWS = PAIR * SEQ
    G = C // (QUADS * PAIR)
    G2 = G // 2
    TCOLS = G2 * QUADS * ROWS
    GC = QUADS * ROWS
    NP = B // SETS
    BG = SETS * G
    SCALE = float(EMB) ** -0.5
    assert 2 * EMB == P and ROWS <= QUAD and SLOTS % 2 == 0 and NP > 3 * SLOTS

    x_dram = x.rearrange("b (g r s) q d -> r (s q) b g d", g=G, r=QUADS)
    out_dram = out.rearrange("b (g r s) q d -> r (s q) b g d", g=G, r=QUADS)

    with ExitStack() as ctx:
        def sb(name, shape):
            return ctx.enter_context(nc.sbuf_tensor(name, shape, F32))

        def psum(name, shape):
            return ctx.enter_context(nc.psum_tensor(name, shape, F32))

        def sem(name):
            return ctx.enter_context(nc.semaphore(name))

        ident = sb("ident", [P, P])
        group_mean = sb("group_mean", [P, P])
        half = sb("half", [P, PAIR])
        half_all = sb("half_all", [P, BG, PAIR])
        wq_sb = sb("wq_sb", [EMB, EMB])
        wk_sb = sb("wk_sb", [EMB, EMB])
        wv_sb = sb("wv_sb", [EMB, EMB])
        bq_sb = sb("bq_sb", [EMB, 1])
        a_bd = sb("a_bd", [P, P])
        wv_bd = sb("wv_bd", [P, P])
        w_col = sb("w_col", [P, 1])
        mix = sb("mix", [P, PAIR, P])
        g_row = sb("g_row", [P, SEQ])
        b_row = sb("b_row", [P, SEQ])
        bv_row = sb("bv_row", [P, EMB])
        g_all = sb("g_all", [P, BG, SEQ])
        b_all = sb("b_all", [P, BG, SEQ])
        bv_all = sb("bv_all", [P, BG, EMB])
        minus_half = sb("minus_half", [P, SETS])

        xs = sb("xs", [P, SLOTS, SETS, G, EMB])
        res = sb("res", [P, SLOTS, SETS, G, EMB])
        xnt = sb("xnt", [P, SETS, TCOLS])
        ht = sb("ht", [P, SETS, TCOLS])
        bns = sb("bns", [P, SETS, 6])
        st = sb("st", [P, SETS, 2])
        st_sq = sb("st_sq", [P, SETS])
        gm = sb("gm", [P, SETS, 2])
        gm_sq = sb("gm_sq", [P, SETS])
        gvar = sb("gvar", [P, SETS])
        gve = sb("gve", [P, SETS])
        gneg = sb("gneg", [P, SETS])
        gscale = sb("gscale", [P, SLOTS, SETS])
        gshift = sb("gshift", [P, SLOTS, SETS])
        en = sb("en", [P, SETS, G2, 2, ROWS])
        esum = sb("esum", [P, BG])
        cent = sb("cent", [P, BG, SEQ])
        cg = sb("cg", [P, BG, SEQ])
        sq = sb("sq", [P, BG, SEQ])
        ssum = sb("ssum", [P, BG])
        lve = sb("lve", [P, BG])
        three = sb("three", [P, BG])
        lln = sb("lln", [P, BG])
        lrs0 = sb("lrs0", [P, BG])
        nw = [sb(f"nw{n}", [P, BG]) for n in range(3)]
        lrs = sb("lrs", [P, BG])
        t1 = sb("t1", [P, BG, SEQ])
        t2 = sb("t2", [P, BG, SEQ])
        tmax = sb("tmax", [P, BG])
        t3 = sb("t3", [P, BG, SEQ])
        ex = sb("ex", [P, BG, SEQ])
        den = sb("den", [P, BG])
        rden = sb("rden", [P, BG])
        rden_s = sb("rden_s", [P, BG, PAIR])
        att = sb("att", [P, BG, QUAD])
        att_bd = sb("att_bd", [P, BG, QUADS, QUAD])
        znt = sb("znt", [P, SETS, G2 * QUADS, QUAD])

        ps_x = [psum(f"ps_x{b}", [P, G2 * QUADS, QUAD]) for b in range(SETS)]
        ps_h = psum("ps_h", [P, 512])
        ps_e = [psum(f"ps_e{h}", [P, SETS * G2, ROWS]) for h in range(2)]
        ps_m = psum("ps_m", [P, BG, SEQ])
        ps_z = psum("ps_z", [P, TCOLS])
        ps_o = psum("ps_o", [P, 512])

        const_loaded = sem("const_loaded")
        cleared = sem("cleared")
        expanded = sem("expanded")
        weights_mm = sem("weights_mm")
        weights_done = sem("weights_done")
        x_loaded = [sem(f"x_loaded{k}") for k in range(SLOTS)]
        stored = [sem(f"stored{k}") for k in range(SLOTS)]
        xt_ready = sem("xt_ready")
        bn_ready = sem("bn_ready")
        agg_ready = sem("agg_ready")
        stsq_ready = sem("stsq_ready")
        st_ready = sem("st_ready")
        gm_mm = sem("gm_mm")
        gm_ready = sem("gm_ready")
        gmsq_ready = sem("gmsq_ready")
        gvar_ready = sem("gvar_ready")
        gve_ready = sem("gve_ready")
        gneg_ready = sem("gneg_ready")
        gscale_ready = sem("gscale_ready")
        gshift_ready = sem("gshift_ready")
        xn_ready = sem("xn_ready")
        h_mm = sem("h_mm")
        ht_ready = sem("ht_ready")
        e_mm = sem("e_mm")
        en_ready = sem("en_ready")
        mix_mm = sem("mix_mm")
        esum_ready = sem("esum_ready")
        cent_ready = sem("cent_ready")
        cg_ready = sem("cg_ready")
        sq_ready = sem("sq_ready")
        ssum_ready = sem("ssum_ready")
        lve_ready = sem("lve_ready")
        lln_ready = sem("lln_ready")
        lrs0_ready = sem("lrs0_ready")
        nw_ready = sem("nw_ready")
        lrs_ready = sem("lrs_ready")
        t1_ready = sem("t1_ready")
        t2_ready = sem("t2_ready")
        tmax_ready = sem("tmax_ready")
        t3_ready = sem("t3_ready")
        ex_ready = sem("ex_ready")
        den_ready = sem("den_ready")
        rden_ready = sem("rden_ready")
        rdens_ready = sem("rdens_ready")
        att_ready = sem("att_ready")
        bd_ready = sem("bd_ready")
        z_mm = sem("z_mm")
        zn_ready = sem("zn_ready")
        o_mm = sem("o_mm")
        xb_ready = sem("xb_ready")
        res_ready = sem("res_ready")

        CLEARED = 7
        CONSTS = 10 + QUADS * PAIR
        LOAD = 16 * QUADS

        block = ctx.enter_context(nc.Block())

        def after(eng, semaphore, value):
            if isinstance(value, int) and value <= 0:
                return
            eng.wait_ge(semaphore, value)

        TURNS = (NP - AHEAD) // SLOTS - 1

        def steps(eng, first, step):
            for p in range(first, SLOTS):
                step(p // SLOTS, p % SLOTS)
            with eng.Fori(1, TURNS + 1) as turn:
                for k in range(SLOTS):
                    step(turn, k)
            for p in range((TURNS + 1) * SLOTS, NP + LAG):
                step(p // SLOTS, p % SLOTS)

        def has(p):
            return not isinstance(p, int) or 0 <= p < NP

        def fills(turn, k):
            return (turn + k // SLOTS + 1) * LOAD

        @block.sync
        def _(sp):
            for dst, src in ((ident[:], ident_c), (group_mean[:], group_c), (half[:], half_c),
                             (wq_sb[:], Wq), (wk_sb[:], Wk), (wv_sb[:], Wv),
                             (bq_sb[:], bq.rearrange("(e a) -> e a", a=1)),
                             (g_row[:], ln_g.partition_broadcast(P)),
                             (b_row[:], ln_b.partition_broadcast(P)),
                             (bv_row[:], bv.partition_broadcast(P))):
                sp.dma_start(dst, src).then_inc(const_loaded, 16)
            sp.wait_ge(cleared, CLEARED)
            for r in range(QUADS):
                for s in range(PAIR):
                    lo = QUAD * r + SEQ * s
                    sp.dma_start(mix[lo:lo + SEQ, s, lo:lo + SEQ],
                                 w_c.rearrange("a l -> l a"),
                                 allow_slow_non_contiguous=True).then_inc(const_loaded, 16)

            def load(p, k):
                for r in range(QUADS):
                    sp.dma_start(xs[QUAD * r:QUAD * r + ROWS, k],
                                 x_dram[r, :, bass.ds(p * SETS, SETS)]).then_inc(x_loaded[k], 16)

            for p in range(SLOTS):
                load(p, p)

            def step(turn, k):
                p, old = turn * SLOTS + k, (k - LAG) % SLOTS
                if has(p - LAG):
                    sp.wait_ge(z_mm, SETS * (p - LAG + 1))
                    sp.wait_ge(xb_ready, p - LAG + 1)
                    if has(p + AHEAD):
                        load(p + AHEAD, old)
                    sp.wait_ge(res_ready, SETS * (p - LAG + 1))
                    for r in range(QUADS):
                        sp.dma_start(out_dram[r, :, bass.ds((p - LAG) * SETS, SETS)],
                                     res[QUAD * r:QUAD * r + ROWS, old]).then_inc(stored[old], 16)

            steps(sp, 0, step)
            for k in range(SLOTS):
                sp.wait_ge(stored[k], len(range(k, NP, SLOTS)) * LOAD)

        @block.gpsimd
        def _(pool):
            nc.gpsimd.memset(xs[:], 0.0).then_inc(cleared, 1)
            nc.gpsimd.memset(mix[:], 0.0).then_inc(cleared, 1)
            nc.gpsimd.memset(att_bd[:], 0.0).then_inc(cleared, 1)
            nc.gpsimd.memset(att[:], 0.0).then_inc(cleared, 1)
            nc.gpsimd.memset(znt[:], 0.0).then_inc(cleared, 1)
            nc.gpsimd.memset(minus_half[:], -0.5).then_inc(cleared, 1)
            nc.gpsimd.memset(three[:], 3.0).then_inc(cleared, 1)
            pool.wait_ge(const_loaded, 16 * CONSTS)
            for n in range(BG):
                nc.gpsimd.tensor_scalar(g_all[:, n], g_row[:], SCALE / 2, None, ALU.mult).then_inc(expanded, 1)
                nc.gpsimd.tensor_scalar(b_all[:, n], b_row[:], SCALE, None, ALU.mult).then_inc(expanded, 1)
                nc.gpsimd.tensor_copy(bv_all[:, n], bv_row[:]).then_inc(expanded, 1)
                nc.gpsimd.tensor_copy(half_all[:, n], half[:]).then_inc(expanded, 1)
            pool.wait_ge(expanded, 4 * BG)

            def over_keys(a):
                return a.unsqueeze(2).to_broadcast([P, BG, SEQ])

            def step(turn, k):
                p, n = turn * SLOTS + k, (k + 1) % SLOTS
                if has(p + 1):
                    pool.wait_ge(gve_ready, p + 2)
                    after(pool, zn_ready, SETS * (p + 2 - SLOTS))
                    nc.gpsimd.tensor_tensor(gscale[:, n], gve[:], minus_half[:],
                                            ALU.pow).then_inc(gscale_ready, 1)
                    pool.wait_ge(gscale_ready, p + 2)
                    pool.wait_ge(gneg_ready, p + 2)
                    nc.gpsimd.tensor_tensor(gshift[:, n], gneg[:], gscale[:, n],
                                            ALU.mult).then_inc(gshift_ready, 1)
                if has(p - 1):
                    pool.wait_ge(rdens_ready, p)
                    after(pool, bd_ready, p - 1)
                    nc.gpsimd.tensor_tensor(
                        att[:, :, 0:ROWS].rearrange("p n (s k) -> p n s k", s=PAIR),
                        ex[:].unsqueeze(2).to_broadcast([P, BG, PAIR, SEQ]),
                        rden_s[:].unsqueeze(3).to_broadcast([P, BG, PAIR, SEQ]),
                        ALU.mult).then_inc(att_ready, 1)
                if has(p):
                    pool.wait_ge(cent_ready, p + 1)
                    after(pool, t1_ready, p)
                    nc.gpsimd.tensor_tensor(cg[:], cent[:], g_all[:], ALU.mult).then_inc(cg_ready, 1)
                    pool.wait_ge(lrs0_ready, p + 1)
                    nc.gpsimd.tensor_tensor(nw[0][:], lrs0[:], lrs0[:], ALU.mult).then_inc(nw_ready, 1)
                    pool.wait_ge(nw_ready, 3 * p + 1)
                    nc.gpsimd.tensor_tensor(nw[1][:], nw[0][:], lve[:], ALU.mult).then_inc(nw_ready, 1)
                    pool.wait_ge(nw_ready, 3 * p + 2)
                    nc.gpsimd.tensor_tensor(nw[2][:], three[:], nw[1][:], ALU.subtract).then_inc(nw_ready, 1)
                    pool.wait_ge(nw_ready, 3 * p + 3)
                    nc.gpsimd.tensor_tensor(lrs[:], nw[2][:], lrs0[:], ALU.mult).then_inc(lrs_ready, 1)
                    pool.wait_ge(cg_ready, p + 1)
                    pool.wait_ge(lrs_ready, p + 1)
                    nc.gpsimd.tensor_tensor(t1[:], cg[:], lrs[:].unsqueeze(2).to_broadcast([P, BG, SEQ]),
                                            ALU.mult).then_inc(t1_ready, 1)
                    pool.wait_ge(t1_ready, p + 1)
                    after(pool, t3_ready, p)
                    nc.gpsimd.tensor_tensor(t2[:], t1[:], b_all[:], ALU.add).then_inc(t2_ready, 1)
                    pool.wait_ge(x_loaded[k], fills(turn, k))
                    after(pool, stored[k], fills(turn - 1, k))
                    nc.gpsimd.tensor_tensor(res[:, k].rearrange("p b g d -> p (b g) d"),
                                            xs[:, k].rearrange("p b g d -> p (b g) d"),
                                            bv_all[:], ALU.add).then_inc(xb_ready, 1)

            steps(pool, -1, step)

        @block.scalar
        def _(act):
            def normalised(dst, src, k, b):
                return nc.scalar.activation(dst, src, ACT.Identity, bias=gshift[:, k, b:b + 1],
                                            scale=gscale[:, k, b:b + 1])

            def h_out(p, b):
                act.wait_ge(h_mm, SETS * p + b + 1)
                nc.scalar.activation(ht[:, b, 0:TCOLS], ps_h[:, 0:TCOLS], ACT.Identity,
                                     bias=w_col[:, 0:1]).then_inc(ht_ready, 1)

            nc.scalar.preload_act_table_set("natural_log_exp_and_others")
            act.wait_ge(cleared, CLEARED)
            act.wait_ge(weights_done, 7)

            def att_x_out(p, old, b):
                act.wait_ge(z_mm, SETS * p + b + 1)
                after(act, o_mm, SETS * (p - 1) + b + 1)
                normalised(znt[:, b, :, 0:ROWS], ps_z[:].rearrange("p (n c) -> p n c", c=ROWS), old, b).then_inc(zn_ready, 1)

            def step(turn, k):
                p, n, old = turn * SLOTS + k, (k + 1) % SLOTS, (k - LAG) % SLOTS
                if has(p - 1):
                    act.wait_ge(t3_ready, p)
                    after(act, att_ready, p - 1)
                    nc.scalar.activation(ex[:], t3[:], ACT.Exp).then_inc(ex_ready, 1)
                if has(p):
                    act.wait_ge(e_mm, p + 1)
                    after(act, mix_mm, p)
                    for h in range(2):
                        nc.scalar.activation(en[:, :, :, h].rearrange("p b g k -> p (b g) k"), ps_e[h][:],
                                             ACT.Copy).then_inc(en_ready, 1)
                if has(p - LAG):
                    att_x_out(p - LAG, old, 0)
                if has(p + 1):
                    act.wait_ge(gshift_ready, p + 2)
                    for b in range(SETS):
                        normalised(xnt[:, b].rearrange("p (n c) -> p n c", c=ROWS),
                                   ps_x[b][:, :, 0:ROWS], n, b).then_inc(xn_ready, 1)
                if has(p):
                    act.wait_ge(cent_ready, p + 1)
                    after(act, ssum_ready, p)
                    nc.scalar.activation(sq[:], cent[:], ACT.Square).then_inc(sq_ready, 1)
                if has(p + 1):
                    h_out(p + 1, 0)
                if has(p - LAG):
                    att_x_out(p - LAG, old, 1)
                if has(p):
                    act.wait_ge(lve_ready, p + 1)
                    nc.scalar.activation(lln[:], lve[:], ACT.Ln).then_inc(lln_ready, 1)
                    act.wait_ge(lln_ready, p + 1)
                    after(act, lrs_ready, p)
                    nc.scalar.activation(lrs0[:], lln[:], ACT.Exp, scale=-0.5).then_inc(lrs0_ready, 1)
                if has(p + 1):
                    h_out(p + 1, 1)

            steps(act, -1, step)

        @block.vector
        def _(dve):
            nc.vector.memset(a_bd[:], 0.0).then_inc(weights_done, 1)
            nc.vector.memset(wv_bd[:], 0.0).then_inc(weights_done, 1)
            for h in range(2):
                nc.vector.memset(ps_e[h][:], 0.0).then_inc(weights_done, 1)
            dve.wait_ge(weights_done, 4)
            dve.wait_ge(weights_mm, 6)
            nc.vector.tensor_copy(w_col[:], ps_h[:, P:P + 1]).then_inc(weights_done, 1)
            for h in range(2):
                r = slice(EMB * h, EMB * h + EMB)
                a = nc.vector.tensor_copy(a_bd[r, r], ps_h[r, 0:EMB])
                v = nc.vector.tensor_copy(wv_bd[r, r], ps_h[r, EMB:2 * EMB])
                v.then_inc(weights_done, 1)

            def result(p, k, b):
                dve.wait_ge(o_mm, SETS * p + b + 1)
                dve.wait_ge(xb_ready, p + 1)
                r = res[:, k, b].rearrange("p g d -> p (g d)")
                nc.vector.tensor_tensor(r, ps_o[:], r, ALU.add).then_inc(res_ready, 1)

            def att_to_diagonal(quads):
                for r in quads:
                    q = slice(QUAD * r, QUAD * r + QUAD)
                    bd = nc.vector.transpose(att_bd[q, :, r, :], att[q, :, :])
                return bd

            def step(turn, k):
                p, old = turn * SLOTS + k, (k - LAG) % SLOTS
                if has(p + 1):
                    for b in range(SETS):
                        dve.wait_ge(xt_ready, SETS * (p + 1) + b + 1)
                        nc.vector.bn_stats(bns[:, b], ps_x[b][:, :, 0:ROWS]).then_inc(bn_ready, 1)
                    dve.wait_ge(bn_ready, SETS * (p + 2))
                if has(p - 1):
                    dve.wait_ge(t2_ready, p)
                    nc.vector.reduce_max(tmax[:], t2[:], AX_X).then_inc(tmax_ready, 1)
                if has(p + 1):
                    for b in range(SETS):
                        nc.vector.bn_aggr(st[:, b], bns[:, b]).then_inc(agg_ready, 1)
                    dve.wait_ge(agg_ready, SETS * (p + 2))
                    nc.vector.tensor_tensor(st_sq[:], st[:, :, 0], st[:, :, 0], ALU.mult).then_inc(stsq_ready, 1)
                    dve.wait_ge(stsq_ready, p + 2)
                    nc.vector.tensor_tensor(st[:, :, 1], st[:, :, 1], st_sq[:], ALU.add).then_inc(st_ready, 1)
                if has(p - 1):
                    dve.wait_ge(tmax_ready, p)
                    after(dve, ex_ready, p - 1)
                    nc.vector.tensor_tensor(t3[:], t2[:], tmax[:].unsqueeze(2).to_broadcast([P, BG, SEQ]),
                                            ALU.subtract).then_inc(t3_ready, 1)
                if has(p + 1):
                    dve.wait_ge(gm_mm, p + 2)
                    nc.vector.tensor_copy(gm[:].rearrange("p b t -> p (b t)"),
                                          ps_h[:, 0:2 * SETS]).then_inc(gm_ready, 1)
                    dve.wait_ge(gm_ready, p + 2)
                    nc.vector.tensor_tensor(gm_sq[:], gm[:, :, 0], gm[:, :, 0], ALU.mult).then_inc(gmsq_ready, 1)
                    dve.wait_ge(gmsq_ready, p + 2)
                    nc.vector.tensor_tensor(gvar[:], gm[:, :, 1], gm_sq[:], ALU.subtract).then_inc(gvar_ready, 1)
                    dve.wait_ge(gvar_ready, p + 2)
                    after(dve, gshift_ready, p + 1)
                    nc.vector.tensor_scalar(gve[:], gvar[:], 0.0, GN_EPS, ALU.max, ALU.add).then_inc(gve_ready, 1)
                    nc.vector.tensor_scalar(gneg[:], gm[:, :, 0], -1.0, None, ALU.mult).then_inc(gneg_ready, 1)
                if has(p - 1):
                    dve.wait_ge(ex_ready, p)
                    nc.vector.reduce_sum(den[:], ex[:], AX_X).then_inc(den_ready, 1)
                    dve.wait_ge(den_ready, p)
                    nc.vector.reciprocal(rden[:], den[:]).then_inc(rden_ready, 1)
                    dve.wait_ge(rden_ready, p)
                    after(dve, att_ready, p - 1)
                    nc.vector.tensor_tensor(rden_s[:], rden[:].unsqueeze(2).to_broadcast([P, BG, PAIR]),
                                            half_all[:], ALU.mult).then_inc(rdens_ready, 1)
                if has(p):
                    dve.wait_ge(mix_mm, p + 1)
                    nc.vector.reduce_sum(esum[:], ps_m[:], AX_X).then_inc(esum_ready, 1)
                    dve.wait_ge(esum_ready, p + 1)
                    after(dve, cg_ready, p)
                    nc.vector.scalar_tensor_tensor(
                        out=cent[:], in0=esum[:].unsqueeze(2).to_broadcast([P, BG, SEQ]), scalar=-1.0 / SEQ,
                        in1=ps_m[:], op0=ALU.mult, op1=ALU.add).then_inc(cent_ready, 1)
                if has(p - 1):
                    dve.wait_ge(att_ready, p)
                    after(dve, z_mm, SETS * (p - 1))
                    att_to_diagonal(range(0, 2))
                if has(p):
                    dve.wait_ge(sq_ready, p + 1)
                    nc.vector.reduce_sum(ssum[:], sq[:], AX_X).then_inc(ssum_ready, 1)
                    dve.wait_ge(ssum_ready, p + 1)
                    after(dve, lrs_ready, p)
                    nc.vector.tensor_scalar(lve[:], ssum[:], 1.0 / SEQ, LN_EPS, ALU.mult,
                                            ALU.add).then_inc(lve_ready, 1)
                if has(p - LAG):
                    result(p - LAG, old, 0)
                if has(p - 1):
                    att_to_diagonal(range(2, QUADS)).then_inc(bd_ready, 1)
                if has(p - LAG):
                    result(p - LAG, old, 1)

            steps(dve, -1, step)

        @block.tensor
        def _(pe):
            pe.wait_ge(const_loaded, 16 * CONSTS)
            for h in range(2):
                r = slice(EMB * h, EMB * h + EMB)
                nc.tensor.matmul(ps_h[r, 0:EMB], wq_sb[:], wk_sb[:], start=True, stop=True).then_inc(weights_mm, 1)
                nc.tensor.matmul(ps_h[r, EMB:2 * EMB], wv_sb[:], ident[0:EMB, 0:EMB],
                                 start=True, stop=True).then_inc(weights_mm, 1)
                nc.tensor.matmul(ps_h[r, P:P + 1], wk_sb[:], bq_sb[:], start=True, stop=True).then_inc(weights_mm, 1)
            pe.wait_ge(weights_done, 7)
            pe.wait_ge(cleared, CLEARED)

            def energies(p):
                for b in range(SETS):
                    for g in range(G2):
                        for r in range(QUADS):
                            c = g * GC + r * ROWS
                            for h in range(2):
                                d = slice(EMB * h, EMB * h + EMB)
                                e = nc.tensor.matmul(ps_e[h][QUAD * r:QUAD * r + ROWS, b * G2 + g, :],
                                                     ht[d, b, c:c + ROWS], xnt[d, b, c:c + ROWS],
                                                     start=True, stop=True)
                e.then_inc(e_mm, 1)

            def transposed(p, loaded, k):
                pe.wait_ge(x_loaded[k], loaded)
                for b in range(SETS):
                    if b == SETS - 1:
                        after(pe, ht_ready, SETS * p)
                    after(pe, xn_ready, SETS * (p - 1) + b + 1)
                    for g in range(G2):
                        t = nc.tensor.transpose(ps_x[b][:, g * QUADS:(g + 1) * QUADS].rearrange("p r c -> p (r c)"),
                                                xs[:, k, b, 2 * g:2 * g + 2].rearrange("p g d -> p (g d)"),
                                                ident[:])
                    t.then_inc(xt_ready, 1)

            def mixing(p):
                pe.wait_ge(en_ready, 2 * (p + 1))
                after(pe, cent_ready, p)
                for s in range(PAIR):
                    m = nc.tensor.matmul(
                        ps_m[:], mix[:, s],
                        en[:].rearrange("p b g h (s k) -> p (b g h) s k", s=PAIR)[:, :, s],
                        start=(s == 0), stop=(s == PAIR - 1))
                m.then_inc(mix_mm, 1)

            def group_means(p):
                pe.wait_ge(st_ready, p + 1)
                after(pe, ht_ready, SETS * p)
                nc.tensor.matmul(ps_h[:, 0:2 * SETS], group_mean[:], st[:].rearrange("p b t -> p (b t)"),
                                 start=True, stop=True).then_inc(gm_mm, 1)

            def hidden(p, b):
                pe.wait_ge(xn_ready, SETS * p + b + 1)
                after(pe, ht_ready, SETS * p + b)
                nc.tensor.matmul(ps_h[:, 0:TCOLS], a_bd[:], xnt[:, b], start=True, stop=True).then_inc(h_mm, 1)

            def attend(p, k, b):
                if b == 0:
                    pe.wait_ge(bd_ready, p + 1)
                after(pe, zn_ready, SETS * p + b)
                for g in range(G2):
                    for h in range(2):
                        z = nc.tensor.matmul(ps_z[EMB * h:EMB * h + EMB, g * GC:(g + 1) * GC],
                                             xs[:, k, b, 2 * g + h],
                                             att_bd[:, b * G + 2 * g + h, :, 0:ROWS],
                                             start=True, stop=True)
                z.then_inc(z_mm, 1)

            def values(p, b):
                pe.wait_ge(zn_ready, SETS * p + b + 1)
                after(pe, res_ready, SETS * p + b)
                for g in range(G2):
                    rows = znt[:, b, g * QUADS:(g + 1) * QUADS].rearrange("p r c -> p (r c)")
                    o = nc.tensor.matmul(ps_o[:, g * P:(g + 1) * P], rows, wv_bd[:], start=True, stop=True)
                o.then_inc(o_mm, 1)

            def step(turn, k):
                p, n, old = turn * SLOTS + k, (k + 1) % SLOTS, (k - LAG) % SLOTS
                if has(p + 1):
                    transposed(p + 1, fills(turn, k + 1), n)
                if has(p):
                    if not has(p + 1):
                        pe.wait_ge(ht_ready, SETS * (p + 1))
                    energies(p)
                if has(p + 1):
                    group_means(p + 1)
                if has(p - LAG):
                    attend(p - LAG, old, 0)
                if has(p):
                    mixing(p)
                if has(p - LAG):
                    attend(p - LAG, old, 1)
                for b in range(SETS):
                    if has(p + 1):
                        hidden(p + 1, b)
                    if has(p - LAG):
                        values(p - LAG, b)

            steps(pe, -1, step)


_INS = ["x", "L0_conv_w_c", "L0_conv_Wq", "L0_conv_bq", "L0_conv_Wk", "L0_conv_bk", "L0_conv_Wv", "L0_conv_bv",
        "L0_conv_ln_g", "L0_conv_ln_b"]


def kernel(**inputs):
    import numpy as _np
    import concourse.bacc as _bacc
    from concourse import mybir as _mybir
    from concourse.bass_utils import run_bass_kernel_spmd as _run

    nc = _bacc.Bacc("TRN2", target_bir_lowering=False, num_devices=1)
    arrays, args = {}, []

    def add(name, a):
        arrays[name] = a
        args.append(nc.dram_tensor(name, a.shape, _mybir.dt.from_np(a.dtype), kind="ExternalInput").ap())

    for name in _INS:
        add(f"in_{name}_dram", _np.ascontiguousarray(inputs[name]))
    seq, emb = inputs["x"].shape[2:]
    p = _np.arange(P)
    add("ident_dram", _np.eye(P, dtype=_np.float32))
    same = (p[:, None] % emb) // 2 == (p[None, :] % emb) // 2
    add("group_dram", same.astype(_np.float32) / _np.float32(4))
    row = p % QUAD
    add("half_dram", _np.stack([(row // seq == s) for s in range(PAIR)], 1).astype(_np.float32))
    shape = inputs["x"].shape
    args.append(nc.dram_tensor("out_0_dram", shape, F32, kind="ExternalOutput").ap())
    conv_preact_kernel(nc, *args)
    r = _run(nc, [arrays], core_ids=[0])
    return r.results[0]["out_0_dram"]
```

```python
from contextlib import ExitStack

import concourse.bass as bass
from concourse import mybir

F32 = mybir.dt.float32
ALU = mybir.AluOpType
ACT = mybir.ActivationFunctionType
AX_X = mybir.AxisListType.X

P = 128
QUAD = 32
QUADS = P // QUAD
PAIR = 2
SETS = 2
SLOTS = 6
LAG = 2
AHEAD = SLOTS - LAG
GN_EPS = 1e-5
LN_EPS = 1e-5


def conv_preact_kernel(nc, x, w_c, Wq, bq, Wk, bk, Wv, bv, ln_g, ln_b, ident_c, group_c, half_c, out):
    B, C, SEQ, EMB = x.shape
    ROWS = PAIR * SEQ
    G = C // (QUADS * PAIR)
    G2 = G // 2
    TCOLS = G2 * QUADS * ROWS
    GC = QUADS * ROWS
    NP = B // SETS
    BG = SETS * G
    SCALE = float(EMB) ** -0.5
    assert 2 * EMB == P and ROWS <= QUAD and SLOTS % 2 == 0 and NP > 3 * SLOTS

    x_dram = x.rearrange("b (g r s) q d -> r (s q) b g d", g=G, r=QUADS)
    out_dram = out.rearrange("b (g r s) q d -> r (s q) b g d", g=G, r=QUADS)

    with ExitStack() as ctx:
        def sb(name, shape):
            return ctx.enter_context(nc.sbuf_tensor(name, shape, F32))

        def psum(name, shape):
            return ctx.enter_context(nc.psum_tensor(name, shape, F32))

        def sem(name):
            return ctx.enter_context(nc.semaphore(name))

        ident = sb("ident", [P, P])
        group_mean = sb("group_mean", [P, P])
        half = sb("half", [P, PAIR])
        half_all = sb("half_all", [P, BG, PAIR])
        wq_sb = sb("wq_sb", [EMB, EMB])
        wk_sb = sb("wk_sb", [EMB, EMB])
        wv_sb = sb("wv_sb", [EMB, EMB])
        bq_sb = sb("bq_sb", [EMB, 1])
        a_bd = sb("a_bd", [P, P])
        wv_bd = sb("wv_bd", [P, P])
        w_col = sb("w_col", [P, 1])
        mix = sb("mix", [P, PAIR, P])
        g_row = sb("g_row", [P, SEQ])
        b_row = sb("b_row", [P, SEQ])
        bv_row = sb("bv_row", [P, EMB])
        g_all = sb("g_all", [P, BG, SEQ])
        b_all = sb("b_all", [P, BG, SEQ])
        bv_all = sb("bv_all", [P, BG, EMB])
        minus_half = sb("minus_half", [P, SETS])

        xs = sb("xs", [P, SLOTS, SETS, G, EMB])
        res = sb("res", [P, SLOTS, SETS, G, EMB])
        xnt = sb("xnt", [P, 2, SETS, TCOLS])
        ht = sb("ht", [P, SETS, TCOLS])
        stats = sb("stats", [P, SETS, 2, 3])
        mean_sq = sb("mean_sq", [P, SETS, 2])
        st = sb("st", [P, SETS, 2])
        gm = sb("gm", [P, SETS, 2])
        gm_sq = sb("gm_sq", [P, SETS])
        gvar = sb("gvar", [P, SETS])
        gve = sb("gve", [P, SETS])
        gneg = sb("gneg", [P, SETS])
        gscale = sb("gscale", [P, SLOTS, SETS])
        gshift = sb("gshift", [P, SLOTS, SETS])
        en = sb("en", [P, SETS, G2, 2, ROWS])
        esum = sb("esum", [P, BG])
        cent = sb("cent", [P, BG, SEQ])
        cg = sb("cg", [P, BG, SEQ])
        sq = sb("sq", [P, BG, SEQ])
        ssum = sb("ssum", [P, BG])
        lve = sb("lve", [P, BG])
        three = sb("three", [P, BG])
        lln = sb("lln", [P, BG])
        lrs0 = sb("lrs0", [P, BG])
        nw = [sb(f"nw{n}", [P, BG]) for n in range(3)]
        lrs = sb("lrs", [P, BG])
        t1 = sb("t1", [P, BG, SEQ])
        t2 = sb("t2", [P, BG, SEQ])
        tmax = sb("tmax", [P, BG])
        t3 = sb("t3", [P, BG, SEQ])
        ex = sb("ex", [P, BG, SEQ])
        den = sb("den", [P, BG])
        rden = sb("rden", [P, BG])
        rden_s = sb("rden_s", [P, BG, PAIR])
        att = sb("att", [P, BG, QUAD])
        att_t = sb("att_t", [P, BG, QUAD])
        att_bd = sb("att_bd", [P, BG, QUADS, QUAD])
        znt = sb("znt", [P, SETS, G2 * QUADS, QUAD])

        ps_x = [psum(f"ps_x{b}", [P, G2 * QUADS, QUAD]) for b in range(SETS)]
        ps_h = psum("ps_h", [P, 512])
        ps_e = [psum(f"ps_e{h}", [P, SETS * G2, ROWS]) for h in range(2)]
        ps_m = psum("ps_m", [P, BG, SEQ])
        ps_z = psum("ps_z", [P, TCOLS])
        ps_o = psum("ps_o", [P, 512])
        h_bank = (ps_h, ps_o)

        const_loaded = sem("const_loaded")
        cleared = sem("cleared")
        expanded = sem("expanded")
        weights_mm = sem("weights_mm")
        weights_done = sem("weights_done")
        x_loaded = [sem(f"x_loaded{k}") for k in range(SLOTS)]
        stored = [sem(f"stored{k}") for k in range(SLOTS)]
        xt_ready = sem("xt_ready")
        bn_ready = sem("bn_ready")
        meansq_ready = sem("meansq_ready")
        stats_ready = sem("stats_ready")
        st_ready = sem("st_ready")
        gm_mm = sem("gm_mm")
        gm_ready = sem("gm_ready")
        gmsq_ready = sem("gmsq_ready")
        gvar_ready = sem("gvar_ready")
        gve_ready = sem("gve_ready")
        gneg_ready = sem("gneg_ready")
        gscale_ready = sem("gscale_ready")
        gshift_ready = sem("gshift_ready")
        xn_ready = sem("xn_ready")
        h_mm = sem("h_mm")
        ht_ready = sem("ht_ready")
        e_mm = sem("e_mm")
        en_ready = sem("en_ready")
        mix_mm = sem("mix_mm")
        esum_ready = sem("esum_ready")
        cent_ready = sem("cent_ready")
        cg_ready = sem("cg_ready")
        sq_ready = sem("sq_ready")
        ssum_ready = sem("ssum_ready")
        lve_ready = sem("lve_ready")
        lln_ready = sem("lln_ready")
        lrs0_ready = sem("lrs0_ready")
        nw_ready = sem("nw_ready")
        lrs_ready = sem("lrs_ready")
        t1_ready = sem("t1_ready")
        t2_ready = sem("t2_ready")
        tmax_ready = sem("tmax_ready")
        t3_ready = sem("t3_ready")
        ex_ready = sem("ex_ready")
        den_ready = sem("den_ready")
        rden_ready = sem("rden_ready")
        rdens_ready = sem("rdens_ready")
        att_ready = sem("att_ready")
        att_t_ready = sem("att_t_ready")
        bd_ready = sem("bd_ready")
        z_mm = sem("z_mm")
        zn_ready = sem("zn_ready")
        o_mm = sem("o_mm")
        xb_ready = sem("xb_ready")
        res_ready = sem("res_ready")

        CLEARED = 7
        CONSTS = 10 + QUADS * PAIR
        LOAD = 16 * QUADS

        block = ctx.enter_context(nc.Block())

        def after(eng, semaphore, value):
            if isinstance(value, int) and value <= 0:
                return
            eng.wait_ge(semaphore, value)

        TURNS = (NP - AHEAD) // SLOTS - 1

        def steps(eng, first, step):
            for p in range(first, SLOTS):
                step(p // SLOTS, p % SLOTS)
            with eng.Fori(1, TURNS + 1) as turn:
                for k in range(SLOTS):
                    step(turn, k)
            for p in range((TURNS + 1) * SLOTS, NP + LAG + 1):
                step(p // SLOTS, p % SLOTS)

        def has(p):
            return not isinstance(p, int) or 0 <= p < NP

        def fills(turn, k):
            return (turn + k // SLOTS + 1) * LOAD

        @block.sync
        def _(sp):
            for dst, src in ((ident[:], ident_c), (group_mean[:], group_c), (half[:], half_c),
                             (wq_sb[:], Wq), (wk_sb[:], Wk), (wv_sb[:], Wv),
                             (bq_sb[:], bq.rearrange("(e a) -> e a", a=1)),
                             (g_row[:], ln_g.partition_broadcast(P)),
                             (b_row[:], ln_b.partition_broadcast(P)),
                             (bv_row[:], bv.partition_broadcast(P))):
                sp.dma_start(dst, src).then_inc(const_loaded, 16)
            sp.wait_ge(cleared, CLEARED)
            for r in range(QUADS):
                for s in range(PAIR):
                    lo = QUAD * r + SEQ * s
                    sp.dma_start(mix[lo:lo + SEQ, s, lo:lo + SEQ],
                                 w_c.rearrange("a l -> l a"),
                                 allow_slow_non_contiguous=True).then_inc(const_loaded, 16)

            def load(p, k):
                for r in range(QUADS):
                    sp.dma_start(xs[QUAD * r:QUAD * r + ROWS, k],
                                 x_dram[r, :, bass.ds(p * SETS, SETS)]).then_inc(x_loaded[k], 16)

            for p in range(SLOTS):
                load(p, p)

            def step(turn, k):
                p, old, older = turn * SLOTS + k, (k - LAG) % SLOTS, (k - LAG - 1) % SLOTS
                if has(p - LAG) and has(p + AHEAD):
                    sp.wait_ge(z_mm, SETS * (p - LAG + 1))
                    sp.wait_ge(xb_ready, p - LAG + 1)
                    load(p + AHEAD, old)
                if has(p - LAG - 1):
                    sp.wait_ge(res_ready, SETS * (p - LAG))
                    for r in range(QUADS):
                        sp.dma_start(out_dram[r, :, bass.ds((p - LAG - 1) * SETS, SETS)],
                                     res[QUAD * r:QUAD * r + ROWS, older]).then_inc(stored[older], 16)

            steps(sp, 0, step)
            for k in range(SLOTS):
                sp.wait_ge(stored[k], len(range(k, NP, SLOTS)) * LOAD)

        @block.gpsimd
        def _(pool):
            nc.gpsimd.memset(xs[:], 0.0).then_inc(cleared, 1)
            nc.gpsimd.memset(mix[:], 0.0).then_inc(cleared, 1)
            nc.gpsimd.memset(att_bd[:], 0.0).then_inc(cleared, 1)
            nc.gpsimd.memset(att[:], 0.0).then_inc(cleared, 1)
            nc.gpsimd.memset(znt[:], 0.0).then_inc(cleared, 1)
            nc.gpsimd.memset(minus_half[:], -0.5).then_inc(cleared, 1)
            nc.gpsimd.memset(three[:], 3.0).then_inc(cleared, 1)
            pool.wait_ge(const_loaded, 16 * CONSTS)
            for n in range(BG):
                nc.gpsimd.tensor_scalar(g_all[:, n], g_row[:], SCALE / 2, None, ALU.mult).then_inc(expanded, 1)
                nc.gpsimd.tensor_scalar(b_all[:, n], b_row[:], SCALE, None, ALU.mult).then_inc(expanded, 1)
                nc.gpsimd.tensor_copy(bv_all[:, n], bv_row[:]).then_inc(expanded, 1)
                nc.gpsimd.tensor_copy(half_all[:, n], half[:]).then_inc(expanded, 1)
            pool.wait_ge(expanded, 4 * BG)

            def over_keys(a):
                return a.unsqueeze(2).to_broadcast([P, BG, SEQ])

            def step(turn, k):
                p, n = turn * SLOTS + k, (k + 1) % SLOTS
                if has(p + 1):
                    pool.wait_ge(gve_ready, p + 2)
                    after(pool, zn_ready, SETS * (p + 2 - SLOTS))
                    nc.gpsimd.tensor_tensor(gscale[:, n], gve[:], minus_half[:],
                                            ALU.pow).then_inc(gscale_ready, 1)
                    pool.wait_ge(gscale_ready, p + 2)
                    pool.wait_ge(gneg_ready, p + 2)
                    nc.gpsimd.tensor_tensor(gshift[:, n], gneg[:], gscale[:, n],
                                            ALU.mult).then_inc(gshift_ready, 1)
                if has(p - 1):
                    pool.wait_ge(rdens_ready, p)
                    after(pool, att_t_ready, p - 1)
                    nc.gpsimd.tensor_tensor(
                        att[:, :, 0:ROWS].rearrange("p n (s k) -> p n s k", s=PAIR),
                        ex[:].unsqueeze(2).to_broadcast([P, BG, PAIR, SEQ]),
                        rden_s[:].unsqueeze(3).to_broadcast([P, BG, PAIR, SEQ]),
                        ALU.mult).then_inc(att_ready, 1)
                if has(p):
                    pool.wait_ge(x_loaded[k], fills(turn, k))
                    after(pool, stored[k], fills(turn - 1, k))
                    nc.gpsimd.tensor_tensor(res[:, k].rearrange("p b g d -> p (b g) d"),
                                            xs[:, k].rearrange("p b g d -> p (b g) d"),
                                            bv_all[:], ALU.add).then_inc(xb_ready, 1)
                    pool.wait_ge(cent_ready, p + 1)
                    after(pool, t1_ready, p)
                    nc.gpsimd.tensor_tensor(cg[:], cent[:], g_all[:], ALU.mult).then_inc(cg_ready, 1)
                    pool.wait_ge(lrs0_ready, p + 1)
                    nc.gpsimd.tensor_tensor(nw[0][:], lrs0[:], lrs0[:], ALU.mult).then_inc(nw_ready, 1)
                    pool.wait_ge(nw_ready, 3 * p + 1)
                    nc.gpsimd.tensor_tensor(nw[1][:], nw[0][:], lve[:], ALU.mult).then_inc(nw_ready, 1)
                    pool.wait_ge(nw_ready, 3 * p + 2)
                    nc.gpsimd.tensor_tensor(nw[2][:], three[:], nw[1][:], ALU.subtract).then_inc(nw_ready, 1)
                    pool.wait_ge(nw_ready, 3 * p + 3)
                    nc.gpsimd.tensor_tensor(lrs[:], nw[2][:], lrs0[:], ALU.mult).then_inc(lrs_ready, 1)
                    pool.wait_ge(cg_ready, p + 1)
                    pool.wait_ge(lrs_ready, p + 1)
                    nc.gpsimd.tensor_tensor(t1[:], cg[:], lrs[:].unsqueeze(2).to_broadcast([P, BG, SEQ]),
                                            ALU.mult).then_inc(t1_ready, 1)
                    pool.wait_ge(t1_ready, p + 1)
                    after(pool, t3_ready, p)
                    nc.gpsimd.tensor_tensor(t2[:], t1[:], b_all[:], ALU.add).then_inc(t2_ready, 1)

            steps(pool, -1, step)

        @block.scalar
        def _(act):
            def normalised(dst, src, k, b):
                return nc.scalar.activation(dst, src, ACT.Identity, bias=gshift[:, k, b:b + 1],
                                            scale=gscale[:, k, b:b + 1])

            def h_out(p, b):
                act.wait_ge(h_mm, SETS * p + b + 1)
                nc.scalar.activation(ht[:, b, 0:TCOLS], h_bank[b][:, 0:TCOLS], ACT.Identity,
                                     bias=w_col[:, 0:1]).then_inc(ht_ready, 1)

            nc.scalar.preload_act_table_set("natural_log_exp_and_others")
            act.wait_ge(cleared, CLEARED)
            act.wait_ge(weights_done, 7)

            def att_x_out(p, old, b):
                act.wait_ge(z_mm, SETS * p + b + 1)
                after(act, o_mm, SETS * (p - 1) + b + 1)
                normalised(znt[:, b, :, 0:ROWS], ps_z[:].rearrange("p (n c) -> p n c", c=ROWS), old, b).then_inc(zn_ready, 1)

            def xn_out(p, n, b):
                if b == 0:
                    act.wait_ge(gshift_ready, p + 1)
                normalised(xnt[:, n % 2, b].rearrange("p (n c) -> p n c", c=ROWS),
                           ps_x[b][:, :, 0:ROWS], n, b).then_inc(xn_ready, 1)

            def to_diagonal(p, quads):
                for r in quads:
                    q = slice(QUAD * r, QUAD * r + QUAD)
                    nc.scalar.activation(att_bd[q, :, r, 0:ROWS], att_t[q, :, 0:ROWS],
                                         ACT.Copy).then_inc(bd_ready, 1)

            def step(turn, k):
                p, n, old = turn * SLOTS + k, (k + 1) % SLOTS, (k - LAG) % SLOTS
                if has(p - LAG):
                    att_x_out(p - LAG, old, 0)
                if has(p - 1):
                    act.wait_ge(t3_ready, p)
                    after(act, att_ready, p - 1)
                    nc.scalar.activation(ex[:], t3[:], ACT.Exp).then_inc(ex_ready, 1)
                if has(p):
                    act.wait_ge(e_mm, p + 1)
                    after(act, mix_mm, p)
                    for h in range(2):
                        nc.scalar.activation(en[:, :, :, h].rearrange("p b g k -> p (b g) k"), ps_e[h][:],
                                             ACT.Copy).then_inc(en_ready, 1)
                if has(p + 1):
                    xn_out(p + 1, n, 0)
                    xn_out(p + 1, n, 1)
                if has(p - LAG):
                    att_x_out(p - LAG, old, 1)
                if has(p + 1):
                    h_out(p + 1, 0)
                if has(p):
                    act.wait_ge(cent_ready, p + 1)
                    after(act, ssum_ready, p)
                    nc.scalar.activation(sq[:], cent[:], ACT.Square).then_inc(sq_ready, 1)
                if has(p - 1):
                    act.wait_ge(att_t_ready, p)
                    after(act, z_mm, SETS * (p - 1))
                    to_diagonal(p - 1, range(0, 1))
                if has(p + 1):
                    h_out(p + 1, 1)
                if has(p):
                    act.wait_ge(lve_ready, p + 1)
                    nc.scalar.activation(lln[:], lve[:], ACT.Ln).then_inc(lln_ready, 1)
                    act.wait_ge(lln_ready, p + 1)
                    after(act, lrs_ready, p)
                    nc.scalar.activation(lrs0[:], lln[:], ACT.Exp, scale=-0.5).then_inc(lrs0_ready, 1)
                if has(p - 1):
                    to_diagonal(p - 1, range(1, QUADS - 1))

            steps(act, -1, step)

        @block.vector
        def _(dve):
            nc.vector.memset(a_bd[:], 0.0).then_inc(weights_done, 1)
            nc.vector.memset(wv_bd[:], 0.0).then_inc(weights_done, 1)
            for h in range(2):
                nc.vector.memset(ps_e[h][:], 0.0).then_inc(weights_done, 1)
            dve.wait_ge(weights_done, 4)
            dve.wait_ge(weights_mm, 6)
            nc.vector.tensor_copy(w_col[:], ps_h[:, P:P + 1]).then_inc(weights_done, 1)
            for h in range(2):
                r = slice(EMB * h, EMB * h + EMB)
                a = nc.vector.tensor_copy(a_bd[r, r], ps_h[r, 0:EMB])
                v = nc.vector.tensor_copy(wv_bd[r, r], ps_h[r, EMB:2 * EMB])
                v.then_inc(weights_done, 1)

            def result(p, k, b):
                dve.wait_ge(o_mm, SETS * p + b + 1)
                dve.wait_ge(xb_ready, p + 1)
                r = res[:, k, b].rearrange("p g d -> p (g d)")
                nc.vector.tensor_tensor(r, ps_o[:], r, ALU.add).then_inc(res_ready, 1)

            def statistics(p, b):
                dve.wait_ge(xt_ready, SETS * p + b + 1)
                nc.vector.bn_stats(stats[:, b].rearrange("p h t -> p (h t)"),
                                   ps_x[b][:, :, 0:ROWS]).then_inc(bn_ready, 1)

            def step(turn, k):
                p, old, older = turn * SLOTS + k, (k - LAG) % SLOTS, (k - LAG - 1) % SLOTS
                if has(p + 1):
                    statistics(p + 1, 1)
                    dve.wait_ge(bn_ready, SETS * (p + 2))
                    nc.vector.tensor_tensor(mean_sq[:], stats[:, :, :, 1], stats[:, :, :, 1],
                                            ALU.mult).then_inc(meansq_ready, 1)
                    dve.wait_ge(meansq_ready, p + 2)
                    nc.vector.scalar_tensor_tensor(
                        out=stats[:, :, :, 2], in0=stats[:, :, :, 2], scalar=2.0 / TCOLS,
                        in1=mean_sq[:], op0=ALU.mult, op1=ALU.add).then_inc(stats_ready, 1)
                    dve.wait_ge(stats_ready, p + 2)
                    nc.vector.tensor_tensor(st[:], stats[:, :, 0, 1:3], stats[:, :, 1, 1:3],
                                            ALU.add).then_inc(st_ready, 1)
                if has(p - LAG - 1):
                    result(p - LAG - 1, older, 1)
                if has(p - 1):
                    dve.wait_ge(t2_ready, p)
                    nc.vector.reduce_max(tmax[:], t2[:], AX_X).then_inc(tmax_ready, 1)
                    dve.wait_ge(tmax_ready, p)
                    after(dve, ex_ready, p - 1)
                    nc.vector.tensor_tensor(t3[:], t2[:], tmax[:].unsqueeze(2).to_broadcast([P, BG, SEQ]),
                                            ALU.subtract).then_inc(t3_ready, 1)
                if has(p + 1):
                    dve.wait_ge(gm_mm, p + 2)
                    nc.vector.tensor_copy(gm[:].rearrange("p b t -> p (b t)"),
                                          ps_h[:, 0:2 * SETS]).then_inc(gm_ready, 1)
                    dve.wait_ge(gm_ready, p + 2)
                    nc.vector.tensor_tensor(gm_sq[:], gm[:, :, 0], gm[:, :, 0], ALU.mult).then_inc(gmsq_ready, 1)
                    dve.wait_ge(gmsq_ready, p + 2)
                    nc.vector.tensor_tensor(gvar[:], gm[:, :, 1], gm_sq[:], ALU.subtract).then_inc(gvar_ready, 1)
                    dve.wait_ge(gvar_ready, p + 2)
                    after(dve, gshift_ready, p + 1)
                    nc.vector.tensor_scalar(gve[:], gvar[:], 0.0, GN_EPS, ALU.max, ALU.add).then_inc(gve_ready, 1)
                    nc.vector.tensor_scalar(gneg[:], gm[:, :, 0], -1.0, None, ALU.mult).then_inc(gneg_ready, 1)
                if has(p - 1):
                    dve.wait_ge(ex_ready, p)
                    nc.vector.reduce_sum(den[:], ex[:], AX_X).then_inc(den_ready, 1)
                    dve.wait_ge(den_ready, p)
                    nc.vector.reciprocal(rden[:], den[:]).then_inc(rden_ready, 1)
                    dve.wait_ge(rden_ready, p)
                    after(dve, att_ready, p - 1)
                    nc.vector.tensor_tensor(rden_s[:], rden[:].unsqueeze(2).to_broadcast([P, BG, PAIR]),
                                            half_all[:], ALU.mult).then_inc(rdens_ready, 1)
                if has(p - LAG):
                    result(p - LAG, old, 0)
                if has(p - 1):
                    dve.wait_ge(att_ready, p)
                    after(dve, bd_ready, QUADS * (p - 1))
                    nc.vector.transpose(att_t[:], att[:]).then_inc(att_t_ready, 1)
                if has(p):
                    dve.wait_ge(mix_mm, p + 1)
                    nc.vector.reduce_sum(esum[:], ps_m[:], AX_X).then_inc(esum_ready, 1)
                    dve.wait_ge(esum_ready, p + 1)
                    after(dve, cg_ready, p)
                    nc.vector.scalar_tensor_tensor(
                        out=cent[:], in0=esum[:].unsqueeze(2).to_broadcast([P, BG, SEQ]), scalar=-1.0 / SEQ,
                        in1=ps_m[:], op0=ALU.mult, op1=ALU.add).then_inc(cent_ready, 1)
                if has(p + 2):
                    statistics(p + 2, 0)
                if has(p - 1):
                    dve.wait_ge(att_t_ready, p)
                    after(dve, z_mm, SETS * (p - 1))
                    q = slice(P - QUAD, P)
                    nc.vector.tensor_copy(att_bd[q, :, QUADS - 1, 0:ROWS],
                                          att_t[q, :, 0:ROWS]).then_inc(bd_ready, 1)
                if has(p):
                    dve.wait_ge(sq_ready, p + 1)
                    nc.vector.reduce_sum(ssum[:], sq[:], AX_X).then_inc(ssum_ready, 1)
                    dve.wait_ge(ssum_ready, p + 1)
                    after(dve, lrs_ready, p)
                    nc.vector.tensor_scalar(lve[:], ssum[:], 1.0 / SEQ, LN_EPS, ALU.mult,
                                            ALU.add).then_inc(lve_ready, 1)

            steps(dve, -2, step)

        @block.tensor
        def _(pe):
            pe.wait_ge(const_loaded, 16 * CONSTS)
            for h in range(2):
                r = slice(EMB * h, EMB * h + EMB)
                nc.tensor.matmul(ps_h[r, 0:EMB], wq_sb[:], wk_sb[:], start=True, stop=True).then_inc(weights_mm, 1)
                nc.tensor.matmul(ps_h[r, EMB:2 * EMB], wv_sb[:], ident[0:EMB, 0:EMB],
                                 start=True, stop=True).then_inc(weights_mm, 1)
                nc.tensor.matmul(ps_h[r, P:P + 1], wk_sb[:], bq_sb[:], start=True, stop=True).then_inc(weights_mm, 1)
            pe.wait_ge(weights_done, 7)
            pe.wait_ge(cleared, CLEARED)

            def energies(p, k, b):
                for g in range(G2):
                    for r in range(QUADS):
                        c = g * GC + r * ROWS
                        for h in range(2):
                            d = slice(EMB * h, EMB * h + EMB)
                            e = nc.tensor.matmul(ps_e[h][QUAD * r:QUAD * r + ROWS, b * G2 + g, :],
                                                 ht[d, b, c:c + ROWS], xnt[d, k % 2, b, c:c + ROWS],
                                                 start=True, stop=True)
                if b == SETS - 1:
                    e.then_inc(e_mm, 1)

            def transposed(p, loaded, k, b):
                if b == 0:
                    pe.wait_ge(x_loaded[k], loaded)
                after(pe, xn_ready, SETS * (p - 1) + b + 1)
                if b == SETS - 1:
                    after(pe, ht_ready, SETS * (p - 1) + 1)
                for g in range(G2):
                    t = nc.tensor.transpose(ps_x[b][:, g * QUADS:(g + 1) * QUADS].rearrange("p r c -> p (r c)"),
                                            xs[:, k, b, 2 * g:2 * g + 2].rearrange("p g d -> p (g d)"),
                                            ident[:])
                t.then_inc(xt_ready, 1)

            def mixing(p):
                pe.wait_ge(en_ready, 2 * (p + 1))
                after(pe, cent_ready, p)
                for s in range(PAIR):
                    m = nc.tensor.matmul(
                        ps_m[:], mix[:, s],
                        en[:].rearrange("p b g h (s k) -> p (b g h) s k", s=PAIR)[:, :, s],
                        start=(s == 0), stop=(s == PAIR - 1))
                m.then_inc(mix_mm, 1)

            def group_means(p):
                pe.wait_ge(st_ready, p + 1)
                after(pe, ht_ready, SETS * p)
                nc.tensor.matmul(ps_h[:, 0:2 * SETS], group_mean[:], st[:].rearrange("p b t -> p (b t)"),
                                 start=True, stop=True).then_inc(gm_mm, 1)

            def hidden(p, k, b):
                pe.wait_ge(xn_ready, SETS * p + b + 1)
                if b == SETS - 1:
                    after(pe, res_ready, SETS * (p - LAG - 1) + 1)
                nc.tensor.matmul(h_bank[b][:, 0:TCOLS], a_bd[:], xnt[:, k % 2, b],
                                 start=True, stop=True).then_inc(h_mm, 1)

            def attend(p, k, b):
                if b == 0:
                    pe.wait_ge(bd_ready, QUADS * (p + 1))
                after(pe, zn_ready, SETS * p + b)
                for g in range(G2):
                    for h in range(2):
                        z = nc.tensor.matmul(ps_z[EMB * h:EMB * h + EMB, g * GC:(g + 1) * GC],
                                             xs[:, k, b, 2 * g + h],
                                             att_bd[:, b * G + 2 * g + h, :, 0:ROWS],
                                             start=True, stop=True)
                z.then_inc(z_mm, 1)

            def values(p, b):
                pe.wait_ge(zn_ready, SETS * p + b + 1)
                after(pe, res_ready, SETS * p + b)
                if b == SETS - 1 and has(p + LAG + 1):
                    pe.wait_ge(ht_ready, SETS * (p + LAG + 2))
                for g in range(G2):
                    rows = znt[:, b, g * QUADS:(g + 1) * QUADS].rearrange("p r c -> p (r c)")
                    o = nc.tensor.matmul(ps_o[:, g * P:(g + 1) * P], rows, wv_bd[:], start=True, stop=True)
                o.then_inc(o_mm, 1)

            def step(turn, k):
                p, old = turn * SLOTS + k, (k - LAG) % SLOTS
                if has(p):
                    if not has(p + 1):
                        pe.wait_ge(ht_ready, SETS * (p + 1))
                    energies(p, k, 0)
                if has(p - LAG - 1):
                    values(p - LAG - 1, 1)
                if has(p - LAG):
                    attend(p - LAG, old, 0)
                if has(p + 1):
                    group_means(p + 1)
                if has(p):
                    energies(p, k, 1)
                if has(p - LAG):
                    values(p - LAG, 0)
                    attend(p - LAG, old, 1)
                if has(p):
                    mixing(p)
                for b in range(SETS):
                    if has(p + 1):
                        hidden(p + 1, k + 1, b)
                    if has(p + 2):
                        transposed(p + 2, fills(turn, k + 2), (k + 2) % SLOTS, b)

            steps(pe, -2, step)


_INS = ["x", "L0_conv_w_c", "L0_conv_Wq", "L0_conv_bq", "L0_conv_Wk", "L0_conv_bk", "L0_conv_Wv", "L0_conv_bv",
        "L0_conv_ln_g", "L0_conv_ln_b"]


def kernel(**inputs):
    import numpy as _np
    import concourse.bacc as _bacc
    from concourse import mybir as _mybir
    from concourse.bass_utils import run_bass_kernel_spmd as _run

    nc = _bacc.Bacc("TRN2", target_bir_lowering=False, num_devices=1)
    arrays, args = {}, []

    def add(name, a):
        arrays[name] = a
        args.append(nc.dram_tensor(name, a.shape, _mybir.dt.from_np(a.dtype), kind="ExternalInput").ap())

    for name in _INS:
        add(f"in_{name}_dram", _np.ascontiguousarray(inputs[name]))
    seq, emb = inputs["x"].shape[2:]
    p = _np.arange(P)
    add("ident_dram", _np.eye(P, dtype=_np.float32))
    same = (p[:, None] % emb) // 2 == (p[None, :] % emb) // 2
    add("group_dram", same.astype(_np.float32) / _np.float32(8))
    row = p % QUAD
    add("half_dram", _np.stack([(row // seq == s) for s in range(PAIR)], 1).astype(_np.float32))
    shape = inputs["x"].shape
    args.append(nc.dram_tensor("out_0_dram", shape, F32, kind="ExternalOutput").ap())
    conv_preact_kernel(nc, *args)
    r = _run(nc, [arrays], core_ids=[0])
    return r.results[0]["out_0_dram"]
```
